# Optimizing a Trainium2 kernel written in Bass

```python
import numpy as np
import jax
import jax.numpy as jnp

def _softmax(x, axis=-1):
    return jax.nn.softmax(x, axis=axis)

def _gelu(x):
    return jax.nn.gelu(x, approximate=True)

def _silu(x):
    return jax.nn.silu(x)

def _sigmoid(x):
    return jax.nn.sigmoid(x)

def _layernorm(x, axis=-1, eps=1e-05):
    m = jnp.mean(x, axis=axis, keepdims=True)
    v = jnp.var(x, axis=axis, keepdims=True)
    return (x - m) / jnp.sqrt(v + eps)

def _scatter_add(tgt, idx, src, axis=0):
    return tgt.at[idx].add(src)

def _segment_sum(src, seg, n):
    return jax.ops.segment_sum(src, seg, n)
kernel_name = 'mk_xattn_seq_d2_seqx_r8_6285d1'

def setup_inputs(seed: int=0):
    np.random.seed(seed)
    _w = jnp.asarray

    def _rec_inputs():
        import jax
        import jax.numpy as jnp
        _rk = jax.random.key(seed)
        x = 0.0002279 + 0.9999 * jax.random.normal(jax.random.fold_in(_rk, 1), (4, 256, 512), jnp.float32)
        _lenS = 256 - jax.random.randint(jax.random.fold_in(_rk, 7), (4,), 0, max(1, 256 // 4) + 1, jnp.int32)
        _lenS2 = 1601 - jax.random.randint(jax.random.fold_in(_rk, 8), (4,), 0, max(1, 1601 // 4) + 1, jnp.int32)
        _ctx_4096P = jax.random.normal(jax.random.fold_in(_rk, 11), (4, 16, 512), jnp.float32)
        _ctx_4096c = jax.random.dirichlet(jax.random.fold_in(_rk, 511), 0.3 * jnp.ones((16,), jnp.float32), (4, 1601))
        _ctx_4096t = jnp.einsum('bsk,bkd->bsd', _ctx_4096c, _ctx_4096P)
        _ctx_4096t = _ctx_4096t * jax.lax.rsqrt(jnp.mean(jnp.square(_ctx_4096t)) + 1e-12) * 0.953939
        ctx_4096 = -0.000702761 + 1.00443 * (_ctx_4096t + 0.3 * jax.random.normal(jax.random.fold_in(_rk, 611), (4, 1601, 512), jnp.float32))
        fside_BxSxS_0 = -0.000132966 + 0.0502041 * jax.random.normal(jax.random.fold_in(_rk, 12), (4, 256, 256), jnp.float32)
        return (x, ctx_4096, fside_BxSxS_0)
    x, ctx_4096, fside_BxSxS_0 = _rec_inputs()

    def _L0_xattn_setup():
        import jax, jax.numpy as jnp
        import numpy as np
        K = 8
        NUM_BLOCKS = 4
        SLOPE = 0.01

        def _lrelu(x):
            return jnp.where(x >= 0, x, SLOPE * x)

        def _knn_indices(xyz, k):
            sq = jnp.sum(xyz * xyz, axis=1)
            d2 = sq[:, :, None] + sq[:, None, :] - 2.0 * jnp.einsum('bdn,bdm->bnm', xyz, xyz)
            _, idx = jax.lax.top_k(-d2, k)
            return idx

        def _group_point(p, idx_t):
            return jnp.take_along_axis(p[:, :, None, :], idx_t, axis=3)
        key = jax.random.key(seed)
        k1, k2, k3, k4 = jax.random.split(key, 4)
        b, n, d = (4, 512, 64)
        xyz = jax.random.normal(k1, (b, 3, n), dtype=jnp.float32)
        points = jax.random.normal(k2, (b, d, n), dtype=jnp.float32)
        w_center = jax.random.normal(k3, (NUM_BLOCKS, d, d), dtype=jnp.float32) * 0.05
        w_neighbor = jax.random.normal(k4, (NUM_BLOCKS, d, d), dtype=jnp.float32) * 0.05
        return {'xyz': xyz, 'points': points, 'w_center': w_center, 'w_neighbor': w_neighbor}
    _L0_xattn_all = _L0_xattn_setup()
    _L0_xattn_in = {k: v for k, v in _L0_xattn_all.items() if k in ()}
    del _L0_xattn_all

    def _L1_xattn_setup():
        import jax, jax.numpy as jnp
        import numpy as np
        K = 8
        NUM_BLOCKS = 4
        SLOPE = 0.01

        def _lrelu(x):
            return jnp.where(x >= 0, x, SLOPE * x)

        def _knn_indices(xyz, k):
            sq = jnp.sum(xyz * xyz, axis=1)
            d2 = sq[:, :, None] + sq[:, None, :] - 2.0 * jnp.einsum('bdn,bdm->bnm', xyz, xyz)
            _, idx = jax.lax.top_k(-d2, k)
            return idx

        def _group_point(p, idx_t):
            return jnp.take_along_axis(p[:, :, None, :], idx_t, axis=3)
        key = jax.random.key(seed)
        k1, k2, k3, k4 = jax.random.split(key, 4)
        b, n, d = (4, 512, 64)
        xyz = jax.random.normal(k1, (b, 3, n), dtype=jnp.float32)
        points = jax.random.normal(k2, (b, d, n), dtype=jnp.float32)
        w_center = jax.random.normal(k3, (NUM_BLOCKS, d, d), dtype=jnp.float32) * 0.05
        w_neighbor = jax.random.normal(k4, (NUM_BLOCKS, d, d), dtype=jnp.float32) * 0.05
        return {'xyz': xyz, 'points': points, 'w_center': w_center, 'w_neighbor': w_neighbor}
    _L1_xattn_all = _L1_xattn_setup()
    _L1_xattn_in = {k: v for k, v in _L1_xattn_all.items() if k in ()}
    del _L1_xattn_all
    return {'x': x, 'ctx_4096': ctx_4096, 'fside_BxSxS_0': fside_BxSxS_0}

def reference(x, ctx_4096, fside_BxSxS_0):
    import jax
    import jax.numpy as jnp

    def _L0_xattn_ref(xyz, points, w_center, w_neighbor):
        import jax, jax.numpy as jnp
        import numpy as np
        K = 8
        NUM_BLOCKS = 4
        SLOPE = 0.01

        def _lrelu(x):
            return jnp.where(x >= 0, x, SLOPE * x)

        def _knn_indices(xyz, k):
            sq = jnp.sum(xyz * xyz, axis=1)
            d2 = sq[:, :, None] + sq[:, None, :] - 2.0 * jnp.einsum('bdn,bdm->bnm', xyz, xyz)
            _, idx = jax.lax.top_k(-d2, k)
            return idx

        def _group_point(p, idx_t):
            return jnp.take_along_axis(p[:, :, None, :], idx_t, axis=3)
        idx = _knn_indices(xyz, K)
        idx_t = jnp.transpose(idx, (0, 2, 1))[:, None, :, :]
        for i in range(NUM_BLOCKS):
            shortcut = points
            p = _lrelu(points)
            g = _group_point(p, idx_t)
            c = jnp.einsum('oi,bin->bon', w_center[i], p)
            gn = jnp.einsum('oi,bikn->bokn', w_neighbor[i], g)
            points = (c + gn.sum(axis=2)) / (K + 1.0) + shortcut
        return points

    def _L1_xattn_ref(xyz, points, w_center, w_neighbor):
        import jax, jax.numpy as jnp
        import numpy as np
        K = 8
        NUM_BLOCKS = 4
        SLOPE = 0.01

        def _lrelu(x):
            return jnp.where(x >= 0, x, SLOPE * x)

        def _knn_indices(xyz, k):
            sq = jnp.sum(xyz * xyz, axis=1)
            d2 = sq[:, :, None] + sq[:, None, :] - 2.0 * jnp.einsum('bdn,bdm->bnm', xyz, xyz)
            _, idx = jax.lax.top_k(-d2, k)
            return idx

        def _group_point(p, idx_t):
            return jnp.take_along_axis(p[:, :, None, :], idx_t, axis=3)
        idx = _knn_indices(xyz, K)
        idx_t = jnp.transpose(idx, (0, 2, 1))[:, None, :, :]
        for i in range(NUM_BLOCKS):
            shortcut = points
            p = _lrelu(points)
            g = _group_point(p, idx_t)
            c = jnp.einsum('oi,bin->bon', w_center[i], p)
            gn = jnp.einsum('oi,bikn->bokn', w_neighbor[i], g)
            points = (c + gn.sum(axis=2)) / (K + 1.0) + shortcut
        return points
    x = _L0_xattn_ref(ctx_4096, x, fside_BxSxS_0, fside_BxSxS_0)
    x = _L1_xattn_ref(ctx_4096, x, fside_BxSxS_0, fside_BxSxS_0)
    return x

_drawn_inputs = setup_inputs


def setup_inputs(seed=0):
    import zlib

    import numpy as np

    out = dict(_drawn_inputs(seed))
    spreads = {}
    factors = {}
    for name, (base, spread) in spreads.items():
        noise = np.random.default_rng([zlib.crc32(name.encode()), seed]).standard_normal(out[name].shape)
        drawn = base * np.exp(spread * noise) if base else spread * noise
        out[name] = jnp.asarray(drawn.astype(out[name].dtype))
    for name, factor in factors.items():
        out[name] = (out[name] * factor).astype(out[name].dtype)
    return out
```

```python
import concourse.bass as bass
from concourse import mybir
from contextlib import ExitStack


def knn_blocks_kernel(nc: bass.Bass, x: bass.AP, ctx_4096: bass.AP, fside: bass.AP, out: bass.AP):
    fp32 = mybir.dt.float32
    fp32r = mybir.dt.float32r
    bf16 = mybir.dt.bfloat16
    ALU = mybir.AluOpType
    ACT = mybir.ActivationFunctionType

    P = 128
    B, C, N = x.shape
    POINT_DIM = ctx_4096.shape[1]
    BLOCKS = fside.shape[0]
    LAYERS = 2 * BLOCKS
    K = 8
    SLOPE = 0.01
    CH = C // P
    NB = N // P
    KT = POINT_DIM // P
    KREST = POINT_DIM - KT * P
    TAKEN = -3.4028234663852886e38

    CHUNKS = [range(0, 4), range(4, 8), range(8, KT + 1)]
    LOADS = [(0, 1, 0), (1, 1, 0), (2, 2, 0), (4, 4, 1), (8, 4, 2), (KT, 1, 2)]
    assert KT == 12 and NB == 4 and CH == 2 and K == 8

    es = ExitStack()
    with es:
        def sb(name, shape, dt):
            return es.enter_context(nc.sbuf_tensor(name, shape, dt))

        def sem(name):
            return es.enter_context(nc.semaphore(name))

        points = sb("points", [P, KT + 1, N], fp32)
        gram = sb("gram", [P, NB, N], fp32)
        dist = sb("dist", [P, NB, N], fp32)
        half_diag = sb("half_diag", [P, N], fp32)
        half_sq = sb("half_sq", [P, NB], fp32)
        top8 = sb("top8", [P, NB, K], fp32)
        marked = sb("marked", [P, NB, N], fp32)
        nbr = sb("nbr", [P, NB, N], bf16)
        adj = sb("adj", [P, B, NB, N], fp32r)
        ident = sb("ident", [P, P], fp32)
        ident_b = sb("ident_b", [P, P], bf16)
        ones = sb("ones", [P, P], fp32)
        eye_wide = sb("eye_wide", [P, 2 * N - P], fp32)
        w_raw = sb("w_raw", [P, BLOCKS, CH, C], fp32)
        w_t = sb("w_t", [P, BLOCKS, CH, C], fp32)
        state = sb("state", [P, B, CH, N], fp32)
        relu = sb("relu", [P, B, CH, N], fp32)
        y_hi = sb("y_hi", [P, 2, NB, C], fp32r)
        y_lo = sb("y_lo", [P, 2, NB, C], fp32r)

        bank = [es.enter_context(nc.psum_tensor(f"bank{i}", [P, N], fp32)) for i in range(8)]
        SQ_BANK, LOW_BANKS, TR_BANKS = 4, (5, 4), (4, 5)
        Y_BANKS = ((0, 1), (2, 3))
        OUT_BANKS = ((6, 7), (4, 5))
        FIRST_OUT_BANKS = ((6, 7), (6, 7))

        points_in = [sem(f"points_in_{n}") for n in range(len(LOADS))]
        w_in = sem("w_in")
        x_in = [sem(f"x_in_{b}") for b in range(B)]
        stored = sem("stored")
        eye_zeroed = sem("eye_zeroed")
        consts_ready = sem("consts_ready")
        w_turned = sem("w_turned")
        w_ready = sem("w_ready")
        chunk_used = sem("chunk_used")
        gram_done = sem("gram_done")
        gram_copied = sem("gram_copied")
        diag_ready = sem("diag_ready")
        sq_row_ready = sem("sq_row_ready")
        dist_ready = sem("dist_ready")
        low_turned = sem("low_turned")
        low_copied = sem("low_copied")
        marked_ready = sem("marked_ready")
        nbr_ready = sem("nbr_ready")
        nbr_turned = sem("nbr_turned")
        adj_ready = sem("adj_ready")
        relu_ready = sem("relu_ready")
        y_done = sem("y_done")
        y_hi_ready = sem("y_hi_ready")
        y_lo_ready = sem("y_lo_ready")
        out_done = sem("out_done")
        state_ready = sem("state_ready")

        block = es.enter_context(nc.Block())

        @block.sync
        def _(sp):
            def load_points(b, n):
                first, tiles, _ = LOADS[n]
                if first < KT:
                    src = ctx_4096[b, 0:KT * P, :].rearrange("(p t) c -> p t c", t=KT)[:, first:first + tiles, :]
                    dst = points[:, first:first + tiles, :]
                else:
                    src = ctx_4096[b, KT * P:POINT_DIM, :]
                    dst = points[0:KREST, KT, :]
                sp.dma_start(dst, src).then_inc(points_in[n], 16)

            for n in range(len(LOADS)):
                load_points(0, n)
            sp.dma_start(w_raw[:, :, :, :], fside.rearrange("l (h p) i -> p l h i", p=P)).then_inc(w_in, 16)
            for b in range(B):
                sp.dma_start(state[:, b, :, :], x[b, :, :].rearrange("(h p) n -> p h n", p=P)).then_inc(x_in[b], 16)
            with sp.Fori(1, B) as b:
                for n, (_, _, chunk) in enumerate(LOADS):
                    if chunk < 2:
                        sp.wait_ge(chunk_used, b * 2 - 1 + chunk)
                    else:
                        sp.wait_ge(gram_done, b * NB)
                    load_points(b, n)
            for b in range(B):
                for h in range(CH):
                    sp.wait_ge(state_ready, 2 * (B * (LAYERS - 1) + b) + h + 1)
                    sp.dma_start(out[b, h * P:(h + 1) * P, :], state[:, b, h, :]).then_inc(stored, 16)
            sp.wait_ge(stored, 16 * B * CH)

        @block.gpsimd
        def _(pool):
            pool.memset(ones[:, :], 1.0).then_inc(consts_ready, 1)
            pool.memset(ident[:, :], 0.0).then_inc(eye_zeroed, 1)
            pool.memset(ident_b[:, :], 0.0).then_inc(eye_zeroed, 1)
            pool.memset(eye_wide[:, :], 0.0).then_inc(eye_zeroed, 1)
            pool.wait_ge(eye_zeroed, 3)
            for tile in (ident[:, :], ident_b[:, :], eye_wide[:, N - P:N]):
                pool.affine_select(out=tile, in_=tile, compare_op=ALU.not_equal, fill=1.0, base=0,
                                   pattern=[[-1, P]], channel_multiplier=1).then_inc(consts_ready, 1)

        @block.tensor
        def _(pe):
            def gram_rows(b, chunk, i, first_batch=False):
                for t in CHUNKS[chunk]:
                    rows = P if t < KT else KREST
                    if i == 0:
                        for n, (first, _, _) in enumerate(LOADS):
                            if first == t:
                                pe.wait_ge(points_in[n], 16 * (b + 1))
                    if t == 0 and not first_batch:
                        pe.wait_ge(gram_copied, (b - 1) * NB + i + 1)
                    mm = nc.tensor.matmul(bank[i][:, 0:N - i * P], points[0:rows, t, i * P:(i + 1) * P],
                                          points[0:rows, t, i * P:N], start=(t == 0), stop=(t == KT))
                if chunk == 2:
                    mm.then_inc(gram_done, 1)
                elif i == NB - 1:
                    mm.then_inc(chunk_used, 1)

            def turn_weights(l):
                if l >= 2:
                    pe.wait_ge(w_ready, l - 1)
                for ih in range(CH):
                    for oh in range(CH):
                        mm = nc.tensor.transpose(bank[6 + l % 2][:, ih * C + oh * P:ih * C + (oh + 1) * P],
                                                 w_raw[:, l, oh, ih * P:(ih + 1) * P], ident[:, :])
                mm.then_inc(w_turned, 1)

            def square_row(b):
                pe.wait_ge(diag_ready, (b + 1) * NB)
                nc.tensor.matmul(bank[SQ_BANK][:, :], ones[:, :], half_diag[:, :],
                                 start=True, stop=True).then_inc(sq_row_ready, 1)

            def turn_distances(b):
                pe.wait_ge(dist_ready, (b + 1) * NB)
                for i, at in ((1, 0), (2, P)):
                    for j in range(i):
                        mm = nc.tensor.transpose(bank[LOW_BANKS[0]][:, at + j * P:at + (j + 1) * P],
                                                 dist[:, j, i * P:(i + 1) * P], ident[:, :])
                mm.then_inc(low_turned, 1)
                for j in range(NB - 1):
                    mm = nc.tensor.transpose(bank[LOW_BANKS[1]][:, j * P:(j + 1) * P],
                                             dist[:, j, (NB - 1) * P:N], ident[:, :])
                mm.then_inc(low_turned, 1)

            def turn_neighbours(b):
                pe.wait_ge(nbr_ready, (b + 1) * NB)
                for g in range(2):
                    pair = bank[TR_BANKS[g]][:, :].bitcast(bf16)
                    for jj in range(2):
                        for i in range(NB):
                            mm = nc.tensor.transpose(pair[:, jj * N + i * P:jj * N + (i + 1) * P],
                                                     nbr[:, i, (2 * g + jj) * P:(2 * g + jj + 1) * P], ident_b[:, :])
                    mm.then_inc(nbr_turned, 1)

            def y_step(s, w, b):
                pe.wait_ge(relu_ready, s + 1)
                for q in range(NB):
                    dst = bank[Y_BANKS[b % 2][q // 2]][:, (q % 2) * C:(q % 2 + 1) * C]
                    for h in range(CH):
                        mm = nc.tensor.matmul(dst, relu[:, b, h, q * P:(q + 1) * P], w_t[:, w, h, :],
                                              start=(h == 0), stop=(h == CH - 1))
                    if q % 2:
                        mm.then_inc(y_done, 1)

            def out_step(s, b, banks):
                for h in range(CH):
                    for q in range(NB):
                        if h == 0 and q % 2 == 0:
                            pe.wait_ge(y_lo_ready, 2 * s + q // 2 + 1)
                        for part in (y_hi, y_lo):
                            mm = nc.tensor.matmul(bank[banks[h]][:, :], part[:, b % 2, q, h * P:(h + 1) * P],
                                                  adj[:, b, q, :], start=(q == 0 and part is y_hi),
                                                  stop=(q == NB - 1 and part is y_lo))
                    mm.then_inc(out_done, 1)

            pe.wait_ge(consts_ready, 4)
            for i in range(NB):
                gram_rows(0, 0, i, first_batch=True)
            for i in range(NB):
                gram_rows(0, 1, i, first_batch=True)
            pe.wait_ge(w_in, 16)
            turn_weights(0)
            turn_weights(1)
            gram_rows(0, 2, 0, first_batch=True)
            turn_weights(2)
            turn_weights(3)
            for i in range(1, NB):
                gram_rows(0, 2, i, first_batch=True)

            with pe.Fori(1, B) as b:
                gram_rows(b, 0, 0)
                square_row(b - 1)
                for i in range(1, NB):
                    gram_rows(b, 0, i)
                turn_distances(b - 1)
                for i in range(NB):
                    gram_rows(b, 1, i)
                gram_rows(b, 2, 0)
                turn_neighbours(b - 1)
                for i in range(1, NB):
                    gram_rows(b, 2, i)

            pe.wait_ge(w_ready, BLOCKS)
            pe.wait_ge(gram_copied, (B - 1) * NB + 2)
            y_step(0, 0, 0)
            square_row(B - 1)
            pe.wait_ge(gram_copied, B * NB)
            y_step(1, 0, 1)
            turn_distances(B - 1)
            out_step(0, 0, FIRST_OUT_BANKS[0])
            y_step(2, 0, 2)
            pe.wait_ge(state_ready, 2)
            out_step(1, 1, FIRST_OUT_BANKS[1])
            y_step(3, 0, 3)
            pe.wait_ge(state_ready, 4)
            out_step(2, 2, FIRST_OUT_BANKS[0])
            turn_neighbours(B - 1)

            with pe.Fori(1, LAYERS) as l:
                for b in range(B):
                    y_step(l * B + b, l % BLOCKS, b)
                    if b == 0:
                        pe.wait_ge(adj_ready, 2 * B)
                    pe.wait_ge(state_ready, 2 * (l * B + b) - 2 * 2)
                    out_step(l * B + b - 1, (b - 1) % B, OUT_BANKS[(b - 1) % 2])
            pe.wait_ge(state_ready, 2 * (LAYERS * B - 2))
            out_step(LAYERS * B - 1, B - 1, OUT_BANKS[1])

        @block.scalar
        def _(act):
            def copy_gram(b, i):
                act.wait_ge(gram_done, b * NB + i + 1)
                nc.scalar.copy(gram[:, i, i * P:N], bank[i][:, 0:N - i * P]).then_inc(gram_copied, 1)

            def copy_low(b):
                act.wait_ge(low_turned, 2 * b + 1)
                nc.scalar.copy(dist[:, 1, 0:P], bank[LOW_BANKS[0]][:, 0:P]).then_inc(low_copied, 1)
                nc.scalar.copy(dist[:, 2, 0:2 * P], bank[LOW_BANKS[0]][:, P:3 * P]).then_inc(low_copied, 1)
                act.wait_ge(low_turned, 2 * b + 2)
                nc.scalar.copy(dist[:, 3, 0:3 * P], bank[LOW_BANKS[1]][:, 0:3 * P]).then_inc(low_copied, 1)

            def copy_adj(b):
                for g in range(2):
                    act.wait_ge(nbr_turned, 2 * b + g + 1)
                    nc.scalar.copy(adj[:, b, 2 * g:2 * g + 2, :],
                                   bank[TR_BANKS[g]][:, :].bitcast(bf16).rearrange("p (j n) -> p j n", j=2))\
                        .then_inc(adj_ready, 1)

            def y_high(s, b):
                for g in range(2):
                    act.wait_ge(y_done, 2 * s + g + 1)
                    nc.scalar.copy(y_hi[:, b % 2, 2 * g:2 * g + 2, :],
                                   bank[Y_BANKS[b % 2][g]][:, :].rearrange("p (q o) -> p q o", q=2))\
                        .then_inc(y_hi_ready, 1)

            for l in range(BLOCKS):
                act.wait_ge(w_turned, l + 1)
                nc.scalar.copy(w_t[:, l, :, :], bank[6 + l % 2][:, :].rearrange("p (h o) -> p h o", h=CH))\
                    .then_inc(w_ready, 1)
            with act.Fori(0, B - 1) as b:
                for i in range(NB):
                    copy_gram(b, i)
                copy_low(b)
                copy_adj(b)
            for i in range(NB):
                copy_gram(B - 1, i)
            y_high(0, 0)
            y_high(1, 1)
            copy_low(B - 1)
            y_high(2, 2)
            y_high(3, 3)
            copy_adj(B - 1)
            with act.Fori(1, LAYERS) as l:
                for b in range(B):
                    y_high(l * B + b, b)

        @block.vector
        def _(dve):
            def make_relu(b):
                nc.vector.scalar_tensor_tensor(relu[:, b, :, :], state[:, b, :, :], SLOPE, state[:, b, :, :],
                                               op0=ALU.mult, op1=ALU.max).then_inc(relu_ready, 1)

            def diagonals(b):
                for i in range(NB):
                    dve.wait_ge(gram_copied, b * NB + i + 1)
                    nc.vector.scalar_tensor_tensor(half_diag[:, i * P:(i + 1) * P], gram[:, i, i * P:(i + 1) * P], -0.5,
                                                   ident[:, :], op0=ALU.mult, op1=ALU.mult,
                                                   accum_out=half_sq[:, i:i + 1]).then_inc(diag_ready, 1)

            def distances(b):
                dve.wait_ge(diag_ready, (b + 1) * NB)
                dve.wait_ge(sq_row_ready, b + 1)
                for i in range(NB):
                    nc.vector.scalar_tensor_tensor(dist[:, i, i * P:N], bank[SQ_BANK][:, i * P:N], half_sq[:, i:i + 1],
                                                   gram[:, i, i * P:N], op0=ALU.add, op1=ALU.add)\
                        .then_inc(dist_ready, 1)
                dve.drain()

            def neighbours(b, i):
                nc.vector.max(top8[:, i, :], dist[:, i, :])
                dve.drain()
                nc.vector.match_replace(marked[:, i, :], top8[:, i, :], dist[:, i, :], TAKEN).then_inc(marked_ready, 1)
                if i < NB - 1:
                    dve.wait_ge(low_copied, b * (NB - 1) + i + 1)
                dve.wait_ge(marked_ready, b * NB + i + 1)
                nc.vector.scalar_tensor_tensor(nbr[:, i, :], marked[:, i, :], TAKEN,
                                               eye_wide[:, N - (i + 1) * P:2 * N - (i + 1) * P],
                                               op0=ALU.is_equal, op1=ALU.add).then_inc(nbr_ready, 1)

            def y_low(s, b):
                for g in range(2):
                    dve.wait_ge(y_hi_ready, 2 * s + g + 1)
                    nc.vector.tensor_tensor(y_lo[:, b % 2, 2 * g:2 * g + 2, :],
                                            bank[Y_BANKS[b % 2][g]][:, :].rearrange("p (q o) -> p q o", q=2),
                                            y_hi[:, b % 2, 2 * g:2 * g + 2, :].bitcast(fp32),
                                            ALU.subtract).then_inc(y_lo_ready, 1)

            def update(s, b, banks):
                for h in range(CH):
                    dve.wait_ge(out_done, 2 * s + h + 1)
                    nc.vector.scalar_tensor_tensor(state[:, b, h, :], bank[banks[h]][:, :], 1.0 / (K + 1),
                                                   state[:, b, h, :], op0=ALU.mult, op1=ALU.add)\
                        .then_inc(state_ready, 1)

            def update_and_relu(s, b, banks):
                update(s, b, banks)
                dve.wait_ge(state_ready, 2 * s + 2)
                make_relu(b)

            for b in range(B):
                dve.wait_ge(x_in[b], 16)
                make_relu(b)
            dve.wait_ge(consts_ready, 4)
            with dve.Fori(0, B - 1) as b:
                diagonals(b)
                distances(b)
                for i in range(NB):
                    neighbours(b, i)

            diagonals(B - 1)
            y_low(0, 0)
            distances(B - 1)
            y_low(1, 1)
            neighbours(B - 1, 0)
            neighbours(B - 1, 1)
            update_and_relu(0, 0, FIRST_OUT_BANKS[0])
            y_low(2, 2)
            neighbours(B - 1, 2)
            update_and_relu(1, 1, FIRST_OUT_BANKS[1])
            y_low(3, 3)
            neighbours(B - 1, 3)
            update_and_relu(2, 2, FIRST_OUT_BANKS[0])

            with dve.Fori(1, LAYERS) as l:
                for b in range(B):
                    y_low(l * B + b, b)
                    update_and_relu(l * B + b - 1, (b - 1) % B, OUT_BANKS[(b - 1) % 2])
            update(LAYERS * B - 1, B - 1, OUT_BANKS[1])


_INS = ['x', 'ctx_4096', 'fside_BxSxS_0']
_OUTS = [((4, 256, 512), 'float32')]


def kernel(**inputs):
    import numpy as _np
    import concourse.bacc as _bacc
    from concourse import mybir as _mybir
    from concourse.bass_utils import run_bass_kernel_spmd as _run

    nc = _bacc.Bacc("TRN2", target_bir_lowering=False, num_devices=1)
    arrays, args = {}, []
    for name in _INS:
        a = _np.ascontiguousarray(inputs[name])
        arrays[f"in_{name}_dram"] = a
        args.append(nc.dram_tensor(f"in_{name}_dram", a.shape, _mybir.dt.from_np(a.dtype), kind="ExternalInput").ap())
    for i, (shape, dtype) in enumerate(_OUTS):
        dt = _mybir.dt.from_np(_np.dtype(dtype))
        args.append(nc.dram_tensor(f"out_{i}_dram", shape, dt, kind="ExternalOutput").ap())
    knn_blocks_kernel(nc, *args)
    r = _run(nc, [arrays], core_ids=[0])
    return r.results[0]["out_0_dram"]
```

```python
import concourse.bass as bass
from concourse import mybir
from contextlib import ExitStack


def knn_blocks_kernel(nc: bass.Bass, x: bass.AP, ctx_4096: bass.AP, fside: bass.AP, out: bass.AP):
    fp32 = mybir.dt.float32
    fp32r = mybir.dt.float32r
    bf16 = mybir.dt.bfloat16
    ALU = mybir.AluOpType
    ACT = mybir.ActivationFunctionType

    P = 128
    B, C, N = x.shape
    POINT_DIM = ctx_4096.shape[1]
    BLOCKS = fside.shape[0]
    LAYERS = 2 * BLOCKS
    K = 8
    SLOPE = 0.01
    CH = C // P
    NB = N // P
    KT = POINT_DIM // P
    HALF = P // 2
    LAST = KT * P + HALF
    TAKEN = -3.4028234663852886e38

    CHUNKS = [range(0, 4), range(4, 8), range(8, KT)]
    LOADS = [(0, 1, 0), (1, 1, 0), (2, 2, 0), (4, 4, 1), (8, 4, 2)]
    assert KT == 12 and LAST == POINT_DIM - 1 and NB == 4 and CH == 2 and K == 8

    es = ExitStack()
    with es:
        def sb(name, shape, dt):
            return es.enter_context(nc.sbuf_tensor(name, shape, dt))

        def sem(name):
            return es.enter_context(nc.semaphore(name))

        points = sb("points", [P, KT, N], fp32)
        rest = sb("rest", [P, N], fp32)
        hi_lo = sb("hi_lo", [P, N], fp32r)
        lo_hi = sb("lo_hi", [P, N], fp32r)
        last_row = sb("last_row", [P, B, N], fp32)
        last_col = sb("last_col", [P, B, NB], fp32)
        gram = sb("gram", [P, NB, N], fp32)
        dist = sb("dist", [P, NB, N], fp32)
        half_diag = sb("half_diag", [P, N], fp32)
        diag_hi = sb("diag_hi", [P, N], fp32r)
        diag_lo = sb("diag_lo", [P, N], fp32r)
        half_sq = sb("half_sq", [P, NB], fp32)
        top8 = sb("top8", [P, NB, K], fp32)
        marked = sb("marked", [P, NB, N], fp32)
        nbr = sb("nbr", [P, NB, N], bf16)
        adj = sb("adj", [P, B, NB, N], fp32r)
        ident = sb("ident", [P, P], fp32)
        ident_b = sb("ident_b", [P, P], bf16)
        ones = sb("ones", [P, P], fp32r)
        eye_wide = sb("eye_wide", [P, 2 * N - P], fp32)
        w_raw = sb("w_raw", [P, BLOCKS, CH, C], fp32)
        w_t = sb("w_t", [P, BLOCKS, CH, C], fp32)
        state = sb("state", [P, B, CH, N], fp32)
        relu = sb("relu", [P, B, CH, N], fp32)
        y_hi = sb("y_hi", [P, 2, NB, C], fp32r)
        y_lo = sb("y_lo", [P, 2, NB, C], fp32r)

        bank = [es.enter_context(nc.psum_tensor(f"bank{i}", [P, N], fp32)) for i in range(8)]
        SQ_BANK, LOW_BANKS, TR_BANKS = 4, (5, 4), (4, 5)
        Y_BANKS = ((0, 1), (2, 3))
        ALL = slice(0, N)
        EVEN_OUT = ((0, ALL, 6), (1, ALL, 7))
        ODD_OUT = ((0, ALL, 4), (1, ALL, 5))
        OUT = (EVEN_OUT, ODD_OUT)
        FIRST_OUT = (EVEN_OUT, EVEN_OUT)
        LAST_OUT = ((0, ALL, 4), (1, slice(0, N // 2), 5), (1, slice(N // 2, N), 0))

        points_in = [sem(f"points_in_{n}") for n in range(len(LOADS))]
        rest_in = sem("rest_in")
        last_in = sem("last_in")
        w_in = sem("w_in")
        x_in = [sem(f"x_in_{b}") for b in range(B)]
        stored = sem("stored")
        eye_zeroed = sem("eye_zeroed")
        consts_ready = sem("consts_ready")
        last_col_ready = sem("last_col_ready")
        rest_hi_ready = sem("rest_hi_ready")
        rest_ready = sem("rest_ready")
        w_turned = sem("w_turned")
        w_ready = sem("w_ready")
        chunk_used = sem("chunk_used")
        gram_done = sem("gram_done")
        gram_ready = sem("gram_ready")
        diag_ready = sem("diag_ready")
        diag_hi_ready = sem("diag_hi_ready")
        diag_split = sem("diag_split")
        sq_row_ready = sem("sq_row_ready")
        dist_ready = sem("dist_ready")
        low_turned = sem("low_turned")
        low_copied = sem("low_copied")
        marked_ready = sem("marked_ready")
        nbr_ready = sem("nbr_ready")
        nbr_turned = sem("nbr_turned")
        adj_ready = sem("adj_ready")
        relu_ready = sem("relu_ready")
        y_done = sem("y_done")
        y_hi_ready = sem("y_hi_ready")
        y_lo_ready = sem("y_lo_ready")
        out_done = sem("out_done")
        state_ready = sem("state_ready")

        block = es.enter_context(nc.Block())

        @block.sync
        def _(sp):
            def load_points(b, n):
                first, tiles, _ = LOADS[n]
                src = ctx_4096[b, 0:KT * P, :].rearrange("(p t) c -> p t c", t=KT)
                sp.dma_start(points[:, first:first + tiles, :], src[:, first:first + tiles, :])\
                  .then_inc(points_in[n], 16)

            def load_rest(b):
                for half in range(2):
                    sp.dma_start(rest[half * HALF:(half + 1) * HALF, :], ctx_4096[b, KT * P:LAST, :])\
                      .then_inc(rest_in, 16)

            for n in range(len(LOADS)):
                load_points(0, n)
            load_rest(0)
            sp.dma_start(w_raw[:, :, :, :], fside.rearrange("l (h p) i -> p l h i", p=P)).then_inc(w_in, 16)
            sp.dma_start(last_row[:, :, :], ctx_4096[:, LAST, :].partition_broadcast(P)).then_inc(last_in, 16)
            for b in range(B):
                sp.dma_start(state[:, b, :, :], x[b, :, :].rearrange("(h p) n -> p h n", p=P)).then_inc(x_in[b], 16)
            with sp.Fori(1, B) as b:
                for n, (_, _, chunk) in enumerate(LOADS):
                    if chunk < 2:
                        sp.wait_ge(chunk_used, b * 2 - 1 + chunk)
                    else:
                        sp.wait_ge(gram_done, b * NB)
                    load_points(b, n)
                load_rest(b)
            stores = [(b, *piece) for b in range(B) for piece in (OUT[b % 2] if b < B - 1 else LAST_OUT)]
            for n, (b, h, cols, _) in enumerate(stores):
                sp.wait_ge(state_ready, 2 * B * (LAYERS - 1) + n + 1)
                sp.dma_start(out[b, h * P:(h + 1) * P, cols], state[:, b, h, cols]).then_inc(stored, 16)
            sp.wait_ge(stored, 16 * len(stores))

        @block.gpsimd
        def _(pool):
            pool.memset(ones[:, :].bitcast(fp32), 1.0).then_inc(consts_ready, 1)
            pool.memset(ident[:, :], 0.0).then_inc(eye_zeroed, 1)
            pool.memset(ident_b[:, :], 0.0).then_inc(eye_zeroed, 1)
            pool.memset(eye_wide[:, :], 0.0).then_inc(eye_zeroed, 1)
            pool.wait_ge(eye_zeroed, 3)
            for tile in (ident[:, :], ident_b[:, :], eye_wide[:, N - P:N]):
                pool.affine_select(out=tile, in_=tile, compare_op=ALU.not_equal, fill=1.0, base=0,
                                   pattern=[[-1, P]], channel_multiplier=1).then_inc(consts_ready, 1)

        @block.tensor
        def _(pe):
            def gram_rows(b, chunk, i, first_batch=False):
                for t in CHUNKS[chunk]:
                    if i == 0:
                        for n, (first, _, _) in enumerate(LOADS):
                            if first == t:
                                pe.wait_ge(points_in[n], 16 * (b + 1))
                    if t == 0 and not first_batch:
                        pe.wait_ge(gram_ready, b * NB - NB + i + 1)
                    mm = nc.tensor.matmul(bank[i][:, 0:N - i * P], points[:, t, i * P:(i + 1) * P],
                                          points[:, t, i * P:N], start=(t == 0), stop=False)
                if chunk == 2:
                    if i == 0:
                        pe.wait_ge(rest_ready, 2 * (b + 1))
                    for moving in (hi_lo, lo_hi):
                        mm = nc.tensor.matmul(bank[i][:, 0:N - i * P], hi_lo[:, i * P:(i + 1) * P],
                                              moving[:, i * P:N], start=False, stop=(moving is lo_hi))
                    mm.then_inc(gram_done, 1)
                elif i == NB - 1:
                    mm.then_inc(chunk_used, 1)

            def turn_weights(l):
                if l >= 2:
                    pe.wait_ge(w_ready, l - 1)
                for ih in range(CH):
                    for oh in range(CH):
                        mm = nc.tensor.transpose(bank[6 + l % 2][:, ih * C + oh * P:ih * C + (oh + 1) * P],
                                                 w_raw[:, l, oh, ih * P:(ih + 1) * P], ident[:, :])
                mm.then_inc(w_turned, 1)

            def square_row(b):
                pe.wait_ge(diag_split, b + 1)
                nc.tensor.matmul(bank[SQ_BANK][:, :], ones[:, :], diag_hi[:, :], start=True, stop=False)
                nc.tensor.matmul(bank[SQ_BANK][:, :], ones[:, :], diag_lo[:, :],
                                 start=False, stop=True).then_inc(sq_row_ready, 1)

            def turn_distances(b):
                pe.wait_ge(dist_ready, (b + 1) * NB)
                for i, at in ((1, 0), (2, P)):
                    for j in range(i):
                        mm = nc.tensor.transpose(bank[LOW_BANKS[0]][:, at + j * P:at + (j + 1) * P],
                                                 dist[:, j, i * P:(i + 1) * P], ident[:, :])
                mm.then_inc(low_turned, 1)
                for j in range(NB - 1):
                    mm = nc.tensor.transpose(bank[LOW_BANKS[1]][:, j * P:(j + 1) * P],
                                             dist[:, j, (NB - 1) * P:N], ident[:, :])
                mm.then_inc(low_turned, 1)

            def turn_neighbours(b):
                pe.wait_ge(nbr_ready, (b + 1) * NB)
                for g in range(2):
                    pair = bank[TR_BANKS[g]][:, :].bitcast(bf16)
                    for jj in range(2):
                        for i in range(NB):
                            mm = nc.tensor.transpose(pair[:, jj * N + i * P:jj * N + (i + 1) * P],
                                                     nbr[:, i, (2 * g + jj) * P:(2 * g + jj + 1) * P], ident_b[:, :])
                    mm.then_inc(nbr_turned, 1)

            def y_step(s, w, b):
                pe.wait_ge(relu_ready, s + 1)
                for q in range(NB):
                    dst = bank[Y_BANKS[b % 2][q // 2]][:, (q % 2) * C:(q % 2 + 1) * C]
                    for h in range(CH):
                        mm = nc.tensor.matmul(dst, relu[:, b, h, q * P:(q + 1) * P], w_t[:, w, h, :],
                                              start=(h == 0), stop=(h == CH - 1))
                    if q % 2:
                        mm.then_inc(y_done, 1)

            def out_step(s, b, pieces):
                for n, (h, cols, to) in enumerate(pieces):
                    for q in range(NB):
                        if n == 0 and q % 2 == 0:
                            pe.wait_ge(y_lo_ready, 2 * s + q // 2 + 1)
                        for part in (y_hi, y_lo):
                            mm = nc.tensor.matmul(bank[to][:, cols], part[:, b % 2, q, h * P:(h + 1) * P],
                                                  adj[:, b, q, cols], start=(q == 0 and part is y_hi),
                                                  stop=(q == NB - 1 and part is y_lo))
                    mm.then_inc(out_done, 1)

            for i in range(NB):
                gram_rows(0, 0, i, first_batch=True)
            for i in range(NB):
                gram_rows(0, 1, i, first_batch=True)
            pe.wait_ge(consts_ready, 4)
            pe.wait_ge(w_in, 16)
            turn_weights(0)
            turn_weights(1)
            gram_rows(0, 2, 0, first_batch=True)
            turn_weights(2)
            turn_weights(3)
            for i in range(1, NB):
                gram_rows(0, 2, i, first_batch=True)

            with pe.Fori(0, B - 1) as before:
                for i in range(2):
                    gram_rows(before + 1, 0, i)
                square_row(before)
                for i in range(2, NB):
                    gram_rows(before + 1, 0, i)
                gram_rows(before + 1, 1, 0)
                turn_distances(before)
                for i in range(1, NB):
                    gram_rows(before + 1, 1, i)
                gram_rows(before + 1, 2, 0)
                turn_neighbours(before)
                for i in range(1, NB):
                    gram_rows(before + 1, 2, i)
                pe.wait_ge(adj_ready, 2 * before + 2)

            pe.wait_ge(w_ready, BLOCKS)
            pe.wait_ge(gram_ready, (B - 1) * NB + 2)
            y_step(0, 0, 0)
            square_row(B - 1)
            pe.wait_ge(gram_ready, B * NB)
            y_step(1, 0, 1)
            turn_distances(B - 1)
            out_step(0, 0, FIRST_OUT[0])
            y_step(2, 0, 2)
            pe.wait_ge(state_ready, 2)
            out_step(1, 1, FIRST_OUT[1])
            y_step(3, 0, 3)
            pe.wait_ge(state_ready, 4)
            out_step(2, 2, FIRST_OUT[0])
            turn_neighbours(B - 1)

            with pe.Fori(1, LAYERS) as l:
                for b in range(B):
                    y_step(l * B + b, l % BLOCKS, b)
                    if b == 0:
                        pe.wait_ge(adj_ready, 2 * B)
                    pe.wait_ge(state_ready, 2 * (l * B + b) - 2 * 2)
                    out_step(l * B + b - 1, (b - 1) % B, OUT[(b - 1) % 2])
            pe.wait_ge(state_ready, 2 * (LAYERS * B - 2))
            out_step(LAYERS * B - 1, B - 1, LAST_OUT)

        @block.scalar
        def _(act):
            def rest_high(b, first_batch=False):
                act.wait_ge(rest_in, 32 * (b + 1))
                if not first_batch:
                    act.wait_ge(gram_done, b * NB)
                for half, tile in enumerate((hi_lo, lo_hi)):
                    at = slice(half * HALF, (half + 1) * HALF)
                    nc.scalar.copy(tile[at, :], rest[at, :]).then_inc(rest_hi_ready, 1)

            def copy_low(b):
                act.wait_ge(low_turned, 2 * b + 1)
                nc.scalar.copy(dist[:, 1, 0:P], bank[LOW_BANKS[0]][:, 0:P]).then_inc(low_copied, 1)
                nc.scalar.copy(dist[:, 2, 0:2 * P], bank[LOW_BANKS[0]][:, P:3 * P]).then_inc(low_copied, 1)
                act.wait_ge(low_turned, 2 * b + 2)
                nc.scalar.copy(dist[:, 3, 0:3 * P], bank[LOW_BANKS[1]][:, 0:3 * P]).then_inc(low_copied, 1)

            def copy_adj(b):
                for g in range(2):
                    act.wait_ge(nbr_turned, 2 * b + g + 1)
                    nc.scalar.copy(adj[:, b, 2 * g:2 * g + 2, :],
                                   bank[TR_BANKS[g]][:, :].bitcast(bf16).rearrange("p (j n) -> p j n", j=2))\
                        .then_inc(adj_ready, 1)

            def y_high(s, b):
                for g in range(2):
                    act.wait_ge(y_done, 2 * s + g + 1)
                    nc.scalar.copy(y_hi[:, b % 2, 2 * g:2 * g + 2, :],
                                   bank[Y_BANKS[b % 2][g]][:, :].rearrange("p (q o) -> p q o", q=2))\
                        .then_inc(y_hi_ready, 1)

            rest_high(0, first_batch=True)
            for l in range(BLOCKS):
                act.wait_ge(w_turned, l + 1)
                nc.scalar.copy(w_t[:, l, :, :], bank[6 + l % 2][:, :].rearrange("p (h o) -> p h o", h=CH))\
                    .then_inc(w_ready, 1)
            with act.Fori(0, B - 1) as b:
                rest_high(b + 1)
                copy_low(b)
                copy_adj(b)
            y_high(0, 0)
            y_high(1, 1)
            copy_low(B - 1)
            y_high(2, 2)
            y_high(3, 3)
            copy_adj(B - 1)
            with act.Fori(1, LAYERS) as l:
                for b in range(B):
                    y_high(l * B + b, b)

        @block.vector
        def _(dve):
            def make_relu(b):
                nc.vector.scalar_tensor_tensor(relu[:, b, :, :], state[:, b, :, :], SLOPE, state[:, b, :, :],
                                               op0=ALU.mult, op1=ALU.max).then_inc(relu_ready, 1)

            def last_columns():
                for b in range(B):
                    for i in range(NB):
                        nc.vector.scalar_tensor_tensor(marked[:, b, i * P:(i + 1) * P], last_row[:, b, i * P:(i + 1) * P], 1.0, ident[:, :],
                                                       op0=ALU.mult, op1=ALU.mult,
                                                       accum_out=last_col[:, b, i:i + 1]).then_inc(last_col_ready, 1)

            def rest_low(b):
                for half, (high, low) in enumerate(((hi_lo, lo_hi), (lo_hi, hi_lo))):
                    at = slice(half * HALF, (half + 1) * HALF)
                    dve.wait_ge(rest_hi_ready, 2 * b + half + 1)
                    nc.vector.tensor_tensor(low[at, :], rest[at, :], high[at, :].bitcast(fp32), ALU.subtract)\
                        .then_inc(rest_ready, 1)

            def gram_and_diagonals(b):
                for i in range(NB):
                    dve.wait_ge(gram_done, b * NB + i + 1)
                    nc.vector.scalar_tensor_tensor(gram[:, i, i * P:N], last_row[:, b, i * P:N], last_col[:, b, i:i + 1],
                                                   bank[i][:, 0:N - i * P], op0=ALU.mult, op1=ALU.add)\
                        .then_inc(gram_ready, 1)
                    dve.wait_ge(gram_ready, b * NB + i + 1)
                    nc.vector.scalar_tensor_tensor(half_diag[:, i * P:(i + 1) * P], gram[:, i, i * P:(i + 1) * P], -0.5,
                                                   ident[:, :], op0=ALU.mult, op1=ALU.mult,
                                                   accum_out=half_sq[:, i:i + 1]).then_inc(diag_ready, 1)
                dve.wait_ge(diag_ready, b * NB + NB)
                nc.vector.tensor_copy(diag_hi[:, :], half_diag[:, :]).then_inc(diag_hi_ready, 1)
                dve.wait_ge(diag_hi_ready, b + 1)
                nc.vector.tensor_tensor(diag_lo[:, :], half_diag[:, :], diag_hi[:, :].bitcast(fp32), ALU.subtract)\
                    .then_inc(diag_split, 1)

            def distances(b):
                dve.wait_ge(sq_row_ready, b + 1)
                for i in range(NB):
                    nc.vector.scalar_tensor_tensor(dist[:, i, i * P:N], bank[SQ_BANK][:, i * P:N], half_sq[:, i:i + 1],
                                                   gram[:, i, i * P:N], op0=ALU.add, op1=ALU.add)\
                        .then_inc(dist_ready, 1)
                dve.drain()

            def neighbours(b, i):
                nc.vector.max(top8[:, i, :], dist[:, i, :])
                dve.drain()
                nc.vector.match_replace(marked[:, i, :], top8[:, i, :], dist[:, i, :], TAKEN).then_inc(marked_ready, 1)
                if i < NB - 1:
                    dve.wait_ge(low_copied, b * (NB - 1) + i + 1)
                dve.wait_ge(marked_ready, b * NB + i + 1)
                nc.vector.scalar_tensor_tensor(nbr[:, i, :], marked[:, i, :], TAKEN,
                                               eye_wide[:, N - (i + 1) * P:2 * N - (i + 1) * P],
                                               op0=ALU.is_equal, op1=ALU.add).then_inc(nbr_ready, 1)

            def y_low(s, b):
                for g in range(2):
                    dve.wait_ge(y_hi_ready, 2 * s + g + 1)
                    nc.vector.tensor_tensor(y_lo[:, b % 2, 2 * g:2 * g + 2, :],
                                            bank[Y_BANKS[b % 2][g]][:, :].rearrange("p (q o) -> p q o", q=2),
                                            y_hi[:, b % 2, 2 * g:2 * g + 2, :].bitcast(fp32),
                                            ALU.subtract).then_inc(y_lo_ready, 1)

            def update(s, b, pieces):
                for n, (h, cols, at) in enumerate(pieces):
                    dve.wait_ge(out_done, 2 * s + n + 1)
                    nc.vector.scalar_tensor_tensor(state[:, b, h, cols], bank[at][:, cols], 1.0 / (K + 1),
                                                   state[:, b, h, cols], op0=ALU.mult, op1=ALU.add)\
                        .then_inc(state_ready, 1)

            def update_and_relu(s, b, pieces):
                update(s, b, pieces)
                dve.wait_ge(state_ready, 2 * s + 2)
                make_relu(b)

            rest_low(0)
            dve.wait_ge(consts_ready, 4)
            dve.wait_ge(last_in, 16)
            last_columns()
            for b in range(B):
                dve.wait_ge(x_in[b], 16)
                make_relu(b)
            dve.wait_ge(last_col_ready, B * NB)
            with dve.Fori(0, B - 1) as b:
                gram_and_diagonals(b)
                rest_low(b + 1)
                distances(b)
                for i in range(NB):
                    neighbours(b, i)

            gram_and_diagonals(B - 1)
            y_low(0, 0)
            distances(B - 1)
            y_low(1, 1)
            neighbours(B - 1, 0)
            neighbours(B - 1, 1)
            update_and_relu(0, 0, FIRST_OUT[0])
            y_low(2, 2)
            neighbours(B - 1, 2)
            update_and_relu(1, 1, FIRST_OUT[1])
            y_low(3, 3)
            neighbours(B - 1, 3)
            update_and_relu(2, 2, FIRST_OUT[0])

            with dve.Fori(1, LAYERS) as l:
                for b in range(B):
                    y_low(l * B + b, b)
                    update_and_relu(l * B + b - 1, (b - 1) % B, OUT[(b - 1) % 2])
            update(LAYERS * B - 1, B - 1, LAST_OUT)


_INS = ['x', 'ctx_4096', 'fside_BxSxS_0']
_OUTS = [((4, 256, 512), 'float32')]


def kernel(**inputs):
    import numpy as _np
    import concourse.bacc as _bacc
    from concourse import mybir as _mybir
    from concourse.bass_utils import run_bass_kernel_spmd as _run

    nc = _bacc.Bacc("TRN2", target_bir_lowering=False, num_devices=1)
    arrays, args = {}, []
    for name in _INS:
        a = _np.ascontiguousarray(inputs[name])
        arrays[f"in_{name}_dram"] = a
        args.append(nc.dram_tensor(f"in_{name}_dram", a.shape, _mybir.dt.from_np(a.dtype), kind="ExternalInput").ap())
    for i, (shape, dtype) in enumerate(_OUTS):
        dt = _mybir.dt.from_np(_np.dtype(dtype))
        args.append(nc.dram_tensor(f"out_{i}_dram", shape, dt, kind="ExternalOutput").ap())
    knn_blocks_kernel(nc, *args)
    r = _run(nc, [arrays], core_ids=[0])
    return r.results[0]["out_0_dram"]
```
